# Optimizing a Trainium2 kernel written in Bass

```python
import numpy as np
import jax
import jax.numpy as jnp

def _softmax(x, axis=-1):
    return jax.nn.softmax(x, axis=axis)

def _gelu(x):
    return jax.nn.gelu(x, approximate=True)

def _silu(x):
    return jax.nn.silu(x)

def _sigmoid(x):
    return jax.nn.sigmoid(x)

def _layernorm(x, axis=-1, eps=1e-05):
    m = jnp.mean(x, axis=axis, keepdims=True)
    v = jnp.var(x, axis=axis, keepdims=True)
    return (x - m) / jnp.sqrt(v + eps)

def _scatter_add(tgt, idx, src, axis=0):
    return tgt.at[idx].add(src)

def _segment_sum(src, seg, n):
    return jax.ops.segment_sum(src, seg, n)
kernel_name = 'mk_lm_tower_d2_tok_ids4096_r4_b8214f'

def setup_inputs(seed: int=0):
    np.random.seed(seed)
    _w = jnp.asarray

    def _rec_inputs():
        import jax
        import jax.numpy as jnp
        _rk = jax.random.key(seed)
        x = jax.random.randint(jax.random.fold_in(_rk, 1), (2, 1024), 0, 12564, jnp.int32)
        return x
    x = _rec_inputs()

    def _L0_tok_setup():
        import jax, jax.numpy as jnp
        import numpy as np
        VOCAB = 50257
        C = 8
        B, T = (4, 1024)
        key = jax.random.key(seed)
        k1, k2, k3 = jax.random.split(key, 3)
        token_ids = jax.random.randint(k1, (B, T), 0, VOCAB)
        dim_embedding = jax.random.normal(k2, (VOCAB, C), dtype=jnp.float32)
        compatibility = jax.random.normal(k3, (C, C), dtype=jnp.float32) * 0.1
        return {'token_ids': token_ids, 'dim_embedding': dim_embedding, 'compatibility': compatibility}
    _L0_tok_all = _L0_tok_setup()
    _L0_tok_in = {k: v for k, v in _L0_tok_all.items() if k in ('dim_embedding', 'compatibility')}
    del _L0_tok_all

    def _L0_attn_setup():
        import jax, jax.numpy as jnp
        import numpy as np
        DIM = 1024
        NUM_HEAD = 32
        NUM_KV_HEAD = 8
        ROPE_THETA = 10000.0
        B, T = (2, 512)

        def apply_rope(x, start_pos=0, theta=ROPE_THETA):
            d = x.shape[-1]
            half = d // 2
            inv_freq = 1.0 / theta ** (jnp.arange(0, half, dtype=jnp.float32) / half)
            pos = jnp.arange(x.shape[1], dtype=jnp.float32) + start_pos
            ang = pos[:, None] * inv_freq[None, :]
            cos = jnp.cos(ang)[None, :, None, :]
            sin = jnp.sin(ang)[None, :, None, :]
            x1, x2 = (x[..., :half], x[..., half:])
            return jnp.concatenate([x1 * cos - x2 * sin, x1 * sin + x2 * cos], axis=-1)
        key = jax.random.key(seed)
        ks = jax.random.split(key, 5)
        scale = 0.02
        X = jax.random.normal(ks[0], (B, T, DIM), dtype=jnp.float32)
        Wq = jax.random.normal(ks[1], (DIM, DIM), dtype=jnp.float32) * scale
        Wk = jax.random.normal(ks[2], (DIM, DIM // NUM_HEAD * NUM_KV_HEAD), dtype=jnp.float32) * scale
        Wv = jax.random.normal(ks[3], (DIM, DIM // NUM_HEAD * NUM_KV_HEAD), dtype=jnp.float32) * scale
        Wo = jax.random.normal(ks[4], (DIM, DIM), dtype=jnp.float32) * scale
        return {'X': X, 'Wq': Wq, 'Wk': Wk, 'Wv': Wv, 'Wo': Wo}
    _L0_attn_all = _L0_attn_setup()
    _L0_attn_in = {k: v for k, v in _L0_attn_all.items() if k in ('Wq', 'Wk', 'Wv', 'Wo')}
    del _L0_attn_all

    def _L0_ffn_setup():
        import jax, jax.numpy as jnp
        import numpy as np
        R = 16
        NUM_EXPERTS = 8
        TOP_K = 2
        LORA_ALPHA = 32
        SCALING = LORA_ALPHA / R
        key = jax.random.key(seed)
        ks = jax.random.split(key, 6)
        d_in, d_out = (1024, 1024)
        x = jax.random.normal(ks[0], (4, 512, d_in), dtype=jnp.float32)
        W_base = jax.random.normal(ks[1], (d_out, d_in), dtype=jnp.float32) * 0.02
        b_base = jax.random.normal(ks[2], (d_out,), dtype=jnp.float32) * 0.02
        W_router = jax.random.normal(ks[3], (NUM_EXPERTS, d_in), dtype=jnp.float32) * 0.01
        A = jax.random.normal(ks[4], (NUM_EXPERTS, R, d_in), dtype=jnp.float32) * 0.02
        B = jax.random.normal(ks[5], (NUM_EXPERTS, d_out, R), dtype=jnp.float32) * 0.02
        return {'x': x, 'W_base': W_base, 'b_base': b_base, 'W_router': W_router, 'A': A, 'B': B}
    _L0_ffn_all = _L0_ffn_setup()
    _L0_ffn_in = {k: v for k, v in _L0_ffn_all.items() if k in ('W_base', 'b_base', 'W_router', 'A', 'B')}
    del _L0_ffn_all

    def _L1_attn_setup():
        import jax, jax.numpy as jnp
        import numpy as np
        H = 32
        HKV = 8
        D = 1024
        HD = D // H
        S = 256
        MASK_OUT = 0.9
        MIN_REMAIN = 128
        THETA = 10000.0

        def rope_tables(seq_len, hd):
            inv_freq = 1.0 / THETA ** (jnp.arange(0, hd, 2, dtype=jnp.float32) / hd)
            t = jnp.arange(seq_len, dtype=jnp.float32)
            freqs = jnp.outer(t, inv_freq)
            emb = jnp.concatenate([freqs, freqs], axis=-1)
            return (jnp.cos(emb), jnp.sin(emb))

        def rotate_half(x):
            x1, x2 = jnp.split(x, 2, axis=-1)
            return jnp.concatenate([-x2, x1], axis=-1)

        def apply_rope(x, cos, sin):
            return x * cos + rotate_half(x) * sin
        key = jax.random.key(seed)
        k0, k1, k2, k3, k4 = jax.random.split(key, 5)
        hidden_states = jax.random.normal(k0, (1, S, D), jnp.float32)
        Wq = jax.random.normal(k1, (D, D), jnp.float32) * 0.02
        Wk = jax.random.normal(k2, (HKV * HD, D), jnp.float32) * 0.02
        Wv = jax.random.normal(k3, (HKV * HD, D), jnp.float32) * 0.02
        Wo = jax.random.normal(k4, (D, D), jnp.float32) * 0.02
        return {'hidden_states': hidden_states, 'Wq': Wq, 'Wk': Wk, 'Wv': Wv, 'Wo': Wo}
    _L1_attn_all = _L1_attn_setup()
    _L1_attn_in = {k: v for k, v in _L1_attn_all.items() if k in ('Wq', 'Wk', 'Wv', 'Wo')}
    del _L1_attn_all

    def _L1_ffn_setup():
        import jax, jax.numpy as jnp
        import numpy as np
        ALPHA = 32
        R = 16
        SCALING = ALPHA / R
        key = jax.random.key(seed)
        k1, k2, k3, k4 = jax.random.split(key, 4)
        B_, S, D = (4, 512, 1024)
        H, r, O = (8, R, 1024)
        x = jax.random.normal(k1, (B_, S, D), dtype=jnp.float32)
        A = jax.random.normal(k2, (H, r, D), dtype=jnp.float32) * 0.02
        Bm = jax.random.normal(k3, (H, O, r), dtype=jnp.float32) * 0.02
        Wr = jax.random.normal(k4, (H, D), dtype=jnp.float32) * 0.02
        br = jnp.zeros((H,), dtype=jnp.float32)
        return {'x': x, 'A': A, 'B': Bm, 'Wr': Wr, 'br': br}
    _L1_ffn_all = _L1_ffn_setup()
    _L1_ffn_in = {k: v for k, v in _L1_ffn_all.items() if k in ('A', 'B', 'Wr', 'br')}
    del _L1_ffn_all
    return {'x': x, 'L0_tok_dim_embedding': _L0_tok_in['dim_embedding'], 'L0_tok_compatibility': _L0_tok_in['compatibility'], 'L0_attn_Wq': _L0_attn_in['Wq'], 'L0_attn_Wk': _L0_attn_in['Wk'], 'L0_attn_Wv': _L0_attn_in['Wv'], 'L0_attn_Wo': _L0_attn_in['Wo'], 'L0_ffn_W_base': _L0_ffn_in['W_base'], 'L0_ffn_b_base': _L0_ffn_in['b_base'], 'L0_ffn_W_router': _L0_ffn_in['W_router'], 'L0_ffn_A': _L0_ffn_in['A'], 'L0_ffn_B': _L0_ffn_in['B'], 'L1_attn_Wq': _L1_attn_in['Wq'], 'L1_attn_Wk': _L1_attn_in['Wk'], 'L1_attn_Wv': _L1_attn_in['Wv'], 'L1_attn_Wo': _L1_attn_in['Wo'], 'L1_ffn_A': _L1_ffn_in['A'], 'L1_ffn_B': _L1_ffn_in['B'], 'L1_ffn_Wr': _L1_ffn_in['Wr'], 'L1_ffn_br': _L1_ffn_in['br']}

def reference(x, L0_tok_dim_embedding, L0_tok_compatibility, L0_attn_Wq, L0_attn_Wk, L0_attn_Wv, L0_attn_Wo, L0_ffn_W_base, L0_ffn_b_base, L0_ffn_W_router, L0_ffn_A, L0_ffn_B, L1_attn_Wq, L1_attn_Wk, L1_attn_Wv, L1_attn_Wo, L1_ffn_A, L1_ffn_B, L1_ffn_Wr, L1_ffn_br):
    import jax
    import jax.numpy as jnp

    def _L0_tok_ref(token_ids, dim_embedding, compatibility):
        import jax, jax.numpy as jnp
        import numpy as np
        VOCAB = 50257
        C = 8
        B, T = (4, 1024)
        dim_probs = jax.nn.softmax(dim_embedding[token_ids], axis=-1)
        compat = jnp.einsum('btc,cd,bsd->bts', dim_probs, compatibility, dim_probs)
        mask_bias = jax.nn.sigmoid(compat) * 2 - 1
        return mask_bias

    def _L0_attn_ref(X, Wq, Wk, Wv, Wo):
        import jax, jax.numpy as jnp
        import numpy as np
        DIM = 1024
        NUM_HEAD = 32
        NUM_KV_HEAD = 8
        ROPE_THETA = 10000.0
        B, T = (2, 512)

        def apply_rope(x, start_pos=0, theta=ROPE_THETA):
            d = x.shape[-1]
            half = d // 2
            inv_freq = 1.0 / theta ** (jnp.arange(0, half, dtype=jnp.float32) / half)
            pos = jnp.arange(x.shape[1], dtype=jnp.float32) + start_pos
            ang = pos[:, None] * inv_freq[None, :]
            cos = jnp.cos(ang)[None, :, None, :]
            sin = jnp.sin(ang)[None, :, None, :]
            x1, x2 = (x[..., :half], x[..., half:])
            return jnp.concatenate([x1 * cos - x2 * sin, x1 * sin + x2 * cos], axis=-1)
        Bs, Ts, C = X.shape
        H, Hkv = (NUM_HEAD, NUM_KV_HEAD)
        dh = C // H
        G = H // Hkv
        Q = apply_rope((X @ Wq).reshape(Bs, Ts, H, dh))
        K = apply_rope((X @ Wk).reshape(Bs, Ts, Hkv, dh))
        V = (X @ Wv).reshape(Bs, Ts, Hkv, dh)
        Qh = Q.transpose(0, 2, 1, 3).reshape(Bs, Hkv, G, Ts, dh)
        Kh = K.transpose(0, 2, 1, 3)
        Vh = V.transpose(0, 2, 1, 3)
        scores = jnp.einsum('bkgtd,bksd->bkgts', Qh, Kh) / jnp.sqrt(jnp.float32(dh))
        causal = jnp.tril(jnp.ones((Ts, Ts), dtype=bool))
        scores = jnp.where(causal[None, None, None], scores, -jnp.inf)
        attn = jax.nn.softmax(scores, axis=-1)
        out = jnp.einsum('bkgts,bksd->bkgtd', attn, Vh)
        out = out.reshape(Bs, H, Ts, dh).transpose(0, 2, 1, 3).reshape(Bs, Ts, C)
        return out @ Wo

    def _L0_ffn_ref(x, W_base, b_base, W_router, A, B):
        import jax, jax.numpy as jnp
        import numpy as np
        R = 16
        NUM_EXPERTS = 8
        TOP_K = 2
        LORA_ALPHA = 32
        SCALING = LORA_ALPHA / R
        orig_shape = x.shape
        d_in = x.shape[-1]
        x_flat = x.reshape(-1, d_in)
        logits = x_flat @ W_router.T
        probs = jax.nn.softmax(logits, axis=-1)
        topk_probs, topk_idx = jax.lax.top_k(probs, TOP_K)
        topk_probs = topk_probs / jnp.sum(topk_probs, axis=-1, keepdims=True)
        onehot = jax.nn.one_hot(topk_idx, NUM_EXPERTS, dtype=x.dtype)
        combine = jnp.einsum('nk,nke->ne', topk_probs, onehot)
        h = jnp.einsum('nd,erd->ner', x_flat, A)
        hw = h * combine[:, :, None]
        expert_out = jnp.einsum('ner,eor->no', hw, B) * SCALING
        base_out = x_flat @ W_base.T + b_base
        out = base_out + expert_out
        return out.reshape(*orig_shape[:-1], W_base.shape[0])

    def _L1_attn_ref(hidden_states, Wq, Wk, Wv, Wo):
        import jax, jax.numpy as jnp
        import numpy as np
        H = 32
        HKV = 8
        D = 1024
        HD = D // H
        S = 256
        MASK_OUT = 0.9
        MIN_REMAIN = 128
        THETA = 10000.0

        def rope_tables(seq_len, hd):
            inv_freq = 1.0 / THETA ** (jnp.arange(0, hd, 2, dtype=jnp.float32) / hd)
            t = jnp.arange(seq_len, dtype=jnp.float32)
            freqs = jnp.outer(t, inv_freq)
            emb = jnp.concatenate([freqs, freqs], axis=-1)
            return (jnp.cos(emb), jnp.sin(emb))

        def rotate_half(x):
            x1, x2 = jnp.split(x, 2, axis=-1)
            return jnp.concatenate([-x2, x1], axis=-1)

        def apply_rope(x, cos, sin):
            return x * cos + rotate_half(x) * sin
        B, Sq, Dm = hidden_states.shape
        dtype = hidden_states.dtype
        neg = jnp.finfo(dtype).min
        q = (hidden_states @ Wq.T).reshape(B, Sq, H, HD).transpose(0, 2, 1, 3)
        k = (hidden_states @ Wk.T).reshape(B, Sq, HKV, HD).transpose(0, 2, 1, 3)
        v = (hidden_states @ Wv.T).reshape(B, Sq, HKV, HD).transpose(0, 2, 1, 3)
        rep = H // HKV
        k = jnp.repeat(k, rep, axis=1)
        v = jnp.repeat(v, rep, axis=1)
        cos, sin = rope_tables(Sq, HD)
        qr = apply_rope(q, cos, sin)
        kr = apply_rope(k, cos, sin)
        draft = jnp.einsum('bhqd,bhkd->bhqk', qr, kr)
        qi = jnp.arange(Sq)
        ki = jnp.arange(Sq)
        causal_future = qi[:, None] < ki[None, :]
        draft = draft + jnp.where(causal_future, neg, jnp.asarray(0.0, dtype))
        num_remain = max(min(Sq, MIN_REMAIN), Sq - int(Sq * MASK_OUT))
        _, draft_indices = jax.lax.top_k(draft, num_remain)
        mask = jnp.full((B, H, Sq, Sq), neg, dtype)
        b_idx = jnp.arange(B)[:, None, None, None]
        h_idx = jnp.arange(H)[None, :, None, None]
        s_idx = jnp.arange(Sq)[None, None, :, None]
        mask = mask.at[b_idx, h_idx, s_idx, draft_indices].set(0.0)
        mask = jnp.where(causal_future[None, None, :, :], neg, mask)
        scores = jnp.einsum('bhqd,bhkd->bhqk', qr, kr) / np.sqrt(HD).astype(np.float32) + mask
        attn = jax.nn.softmax(scores, axis=-1)
        out = jnp.einsum('bhqk,bhkd->bhqd', attn, v)
        out = out.transpose(0, 2, 1, 3).reshape(B, Sq, Dm)
        return out @ Wo.T

    def _L1_ffn_ref(x, A, B, Wr, br):
        import jax, jax.numpy as jnp
        import numpy as np
        ALPHA = 32
        R = 16
        SCALING = ALPHA / R
        H = A.shape[0]
        router_logits = jnp.einsum('bsd,hd->bsh', x, Wr) + br
        scores = H * jax.nn.softmax(router_logits, axis=-1)
        low = jnp.einsum('bsd,hrd->bshr', x, A)
        out = jnp.einsum('bshr,hor,bsh->bso', low, B, scores)
        return SCALING * out
    h = _L0_tok_ref(x, L0_tok_dim_embedding, L0_tok_compatibility)
    h = h + _L0_attn_ref(_layernorm(h, axis=-1), L0_attn_Wq, L0_attn_Wk, L0_attn_Wv, L0_attn_Wo)
    h = h + _L0_ffn_ref(_layernorm(h, axis=-1), L0_ffn_W_base, L0_ffn_b_base, L0_ffn_W_router, L0_ffn_A, L0_ffn_B)
    h = h + _L1_attn_ref(_layernorm(h, axis=-1), L1_attn_Wq, L1_attn_Wk, L1_attn_Wv, L1_attn_Wo)
    h = h + _L1_ffn_ref(_layernorm(h, axis=-1), L1_ffn_A, L1_ffn_B, L1_ffn_Wr, L1_ffn_br)
    return h

_drawn_inputs = setup_inputs


def setup_inputs(seed=0):
    import zlib

    import numpy as np

    out = dict(_drawn_inputs(seed))
    spreads = {'L1_ffn_br': (0.0, 0.278)}
    factors = {'L1_attn_Wq': 4.054, 'L1_attn_Wk': 4.584}
    for name, (base, spread) in spreads.items():
        noise = np.random.default_rng([zlib.crc32(name.encode()), seed]).standard_normal(out[name].shape)
        drawn = base * np.exp(spread * noise) if base else spread * noise
        out[name] = jnp.asarray(drawn.astype(out[name].dtype))
    for name, factor in factors.items():
        out[name] = (out[name] * factor).astype(out[name].dtype)
    return out
```

```python
from contextlib import ExitStack
from itertools import count

import concourse.bass as bass
from concourse import mybir

ALU = mybir.AluOpType
ACT = mybir.ActivationFunctionType
AX_X = mybir.AxisListType.X
F32 = mybir.dt.float32
BF16 = mybir.dt.bfloat16
I32 = mybir.dt.int32
U32 = mybir.dt.uint32
ds = bass.ds

P = 128
B = 2
T = 1024
D = 1024
NT = B * T // P
TT = T // P
KD = D // P
H = 32
HKV = 8
G = H // HKV
DH = D // H
HALF = DH // 2
QK = (H + HKV) * DH
QKV = QK + HKV * DH
NQK = QK // P
SPLITS = 3
Q_PARTS = ((0, 0, 0, 1), (1, 2, 1, 2))
K_PARTS = ((0, 1, 2, 0), (1, 0, 2, 1))
BANK = 512
C = 8
NE = 8
R = 16
ER = NE * R
SCALE = float(DH) ** -0.5
EPS = 1e-5
LORA = 2.0
KEEP = 128
AIM = KEEP - 3.5
MASKED = -1e30
TAKEN = -3e38
SEG = TT * (TT + 1) // 2 * P
NS = 2 * (TT - 1)
PASSES = 5


def off(i):
    return P * i * (i + 1) // 2


def chunks(n, size=BANK):
    return [(a, min(size, n - a)) for a in range(0, n, size)]


def over_tiles(eng, step, peeled=1):
    for j in range(peeled):
        step(j, j % 2, j == 0, False)
    with eng.Fori(0, (NT - 1 - peeled) // 2) as r:
        for c in (peeled, peeled + 1):
            step(r * 2 + c, c % 2, False, False)
    step(NT - 1, (NT - 1) % 2, False, True)


def inv_sqrt(nc, dve, x, x_half, tmp, y, steps=3):
    nc.vector.tensor_scalar(y.bitcast(I32), x.bitcast(I32), -0.5, float(0x5F3759DF), ALU.mult, ALU.add)
    dve.drain()
    for _ in range(steps):
        nc.vector.tensor_tensor(tmp, y, y, ALU.mult)
        dve.drain()
        nc.vector.tensor_tensor(tmp, tmp, x_half, ALU.mult)
        dve.drain()
        nc.vector.scalar_tensor_tensor(out=y, in0=tmp, scalar=1.5, in1=y, op0=ALU.add, op1=ALU.mult)
        dve.drain()


def layer_norm(nc, dve, x, stats, mv, rstd, out, gather=True):
    if gather:
        nc.vector.bn_stats(stats[:, 0:6], x[:, 0:BANK])
        nc.vector.bn_stats(stats[:, 6:12], x[:, BANK:D])
    dve.drain()
    nc.vector.bn_aggr(mv, stats)
    dve.drain()
    v, v_half, tmp, y = (rstd[:, k:k + 1] for k in range(4))
    nc.vector.tensor_scalar(v, mv[:, 1:2], EPS, None, ALU.add)
    nc.vector.tensor_scalar(v_half, mv[:, 1:2], EPS, -0.5, ALU.add, ALU.mult)
    dve.drain()
    inv_sqrt(nc, dve, v, v_half, tmp, y)
    return nc.vector.tensor_scalar(out, x, mv[:, 0:1], y, ALU.subtract, ALU.mult)


def token_map(nc, ids, embedding, compat, const, h_dram):
    with ExitStack() as ctx:
        sb = lambda n, s, d=F32: ctx.enter_context(nc.sbuf_tensor(n, s, d))
        ps = lambda n, s: ctx.enter_context(nc.psum_tensor(n, s, F32))
        sem = lambda n: ctx.enter_context(nc.semaphore(n))
        idx = sb("tok_idx", [P, NT], I32)
        rows = sb("tok_rows", [P, NT, C])
        prob = sb("tok_prob", [P, NT, C])
        top = sb("tok_top", [P, NT])
        total = sb("tok_total", [P, NT])
        ident = sb("tok_ident", [P, P])
        cmat = sb("tok_compat", [C, C])
        pT = sb("tok_pT", [C, B * T])
        pcT = sb("tok_pcT", [C, B * T])
        hout = sb("tok_h", [P, 4, D])
        ps_t = ps("tok_ps_t", [P, 4 * BANK])
        ps_h = ps("tok_ps_h", [P, 2, D])
        ids_in, const_in, rows_in = sem("t_ids_in"), sem("t_const_in"), sem("t_rows_in")
        shifted, exped, prob_ready = sem("t_shifted"), sem("t_exped"), sem("t_prob_ready")
        pT_done, pT_ready, pc_done, pc_ready = sem("t_pT_done"), sem("t_pT_ready"), sem("t_pc_done"), sem("t_pc_ready")
        map_done, h_ready, stored = sem("t_map_done"), sem("t_h_ready"), [sem(f"t_stored{k}") for k in range(4)]
        with nc.Block() as block:

            @block.gpsimd
            def _(pool):
                pool.dma_start(idx[:, :], ids).then_inc(ids_in, 16)
                pool.wait_ge(ids_in, 16)
                for j in range(NT):
                    nc.gpsimd.indirect_dma_start(
                        out=rows[:, j, :], out_offset=None, in_=embedding,
                        in_offset=bass.IndirectOffsetOnAxis(ap=idx[:, j:j + 1].bitcast(U32), axis=0),
                    ).then_inc(rows_in, 16)

            @block.sync
            def _(sp):
                sp.dma_start(ident[:, :], const["ident"]).then_inc(const_in, 16)
                sp.dma_start(cmat[:, :], compat).then_inc(const_in, 16)
                for j in range(NT):
                    sp.wait_ge(h_ready, j + 1)
                    sp.dma_start(h_dram[j * P:(j + 1) * P, :], hout[:, j % 4, :]).then_inc(stored[j % 4], 16)
                for k in range(4):
                    sp.wait_ge(stored[k], 16 * (NT // 4))

            @block.vector
            def _(dve):
                dve.wait_ge(rows_in, 16 * NT)
                nc.vector.tensor_reduce(top[:, :], rows[:, :, :], AX_X, ALU.max)
                dve.drain()
                nc.vector.tensor_tensor(prob[:, :, :], rows[:, :, :], top[:, :].unsqueeze(2).to_broadcast([P, NT, C]),
                                        ALU.subtract).then_inc(shifted, 1)
                dve.wait_ge(exped, 1)
                nc.vector.tensor_reduce(total[:, :], rows[:, :, :], AX_X, ALU.add)
                dve.drain()
                nc.vector.reciprocal(top[:, :], total[:, :])
                dve.drain()
                nc.vector.tensor_tensor(prob[:, :, :], rows[:, :, :], top[:, :].unsqueeze(2).to_broadcast([P, NT, C]),
                                        ALU.mult).then_inc(prob_ready, 1)
                for q in range(4):
                    dve.wait_ge(pT_done, q + 1)
                    nc.vector.tensor_copy(pT[:, q * BANK:(q + 1) * BANK],
                                          ps_t[0:C, q * BANK:(q + 1) * BANK]).then_inc(pT_ready, 1)
                for q in range(4):
                    dve.wait_ge(pc_done, q + 1)
                    nc.vector.tensor_copy(pcT[:, q * BANK:(q + 1) * BANK],
                                          ps_t[0:C, q * BANK:(q + 1) * BANK]).then_inc(pc_ready, 1)

            @block.tensor
            def _(pe):
                pe.wait_ge(const_in, 32)
                pe.wait_ge(prob_ready, 1)
                for j in range(NT):
                    m = nc.tensor.transpose(ps_t[0:C, j * P:(j + 1) * P], prob[:, j, :], ident[:, :])
                    if j % 4 == 3:
                        m.then_inc(pT_done, 1)
                for q in range(4):
                    pe.wait_ge(pT_ready, q + 1)
                    nc.tensor.matmul(ps_t[0:C, q * BANK:(q + 1) * BANK], cmat[:, :], pT[:, q * BANK:(q + 1) * BANK],
                                     start=True, stop=True).then_inc(pc_done, 1)
                pe.wait_ge(pc_ready, 4)
                for j in range(NT):
                    if j >= 2:
                        pe.wait_ge(h_ready, j - 1)
                    for a, n in chunks(T):
                        s0 = (j // TT) * T + a
                        m = nc.tensor.matmul(ps_h[:, j % 2, a:a + n], pcT[:, j * P:(j + 1) * P], pT[:, s0:s0 + n],
                                             start=True, stop=True)
                    m.then_inc(map_done, 1)

            @block.scalar
            def _(act):
                act.wait_ge(shifted, 1)
                nc.scalar.activation(rows[:, :, :], prob[:, :, :], ACT.Exp).then_inc(exped, 1)
                for j in range(NT):
                    act.wait_ge(map_done, j + 1)
                    if j >= 4:
                        act.wait_ge(stored[j % 4], 16 * (j // 4))
                    nc.scalar.activation(hout[:, j % 4, :], ps_h[:, j % 2, :], ACT.Tanh,
                                         scale=0.5).then_inc(h_ready, 1)


NUMBERS = count()


def wait_alone(eng, sem, value, met, met_value):
    if isinstance(value, int):
        eng.wait_ge(sem, value)
        return
    with eng.register(f"target_{next(NUMBERS)}") as target:
        eng.reg_mov(target, value)
        eng.wait_ge(met, met_value)
        eng.wait_ge(sem, target)


def project(nc, tag, w_in, use, w_dram, const, h_dram, qk_dram, v_dram):
    with ExitStack() as ctx:
        sb = lambda n, s, d=F32: ctx.enter_context(nc.sbuf_tensor(tag + n, s, d))
        ps = lambda n, s: ctx.enter_context(nc.psum_tensor(tag + n, s, F32))
        sem = lambda n: ctx.enter_context(nc.semaphore(tag + n))
        w = sb("w", [P, KD, QKV])
        ident = sb("ident", [P, P])
        rope = sb("rope", [P, TT * 2 * DH])
        h = sb("h", [P, 2, D])
        hn = sb("hn", [P, 2, D])
        hT = sb("hT", [P, 2, KD * P])
        rot = sb("rot", [P, 2, QK])
        half = sb("half", [P, 3, BANK])
        v = sb("v", [P, 2, HKV * DH])
        part = sb("part", [P, 2, SPLITS * QK], BF16)
        qkT = sb("qkT", [P, 2, SPLITS * QK], BF16)
        ident_b = sb("ident_b", [P, P], BF16)
        stats, mv, rstd = sb("stats", [P, 2, 12]), sb("mv", [P, 2, 2]), sb("rstd", [P, 2, 4])
        ps_qkv = ps("ps_qkv", [P, 3 * BANK])
        ps_h = ps("ps_h", [P, 2 * BANK])
        ps_qk = ctx.enter_context(nc.psum_tensor(tag + "ps_qk", [P, 3, 2 * BANK], BF16))
        const_in = sem("const_in")
        h_in = [sem("h_in0"), sem("h_in1")]
        hn_ready, hT_done, hT_ready = sem("hn_ready"), sem("hT_done"), sem("hT_ready")
        qkv_done, rope_done, v_ready = sem("qkv_done"), sem("rope_done"), sem("v_ready")
        qkT_done, qkT_ready = sem("qkT_done"), sem("qkT_ready")
        parts_ready, const_ready = sem("parts_ready"), sem("const_ready")
        TURNS = chunks(SPLITS * QK, 2 * BANK)
        NQ = len(TURNS)
        qk_out, v_out = [sem("qk_out0"), sem("qk_out1")], [sem("v_out0"), sem("v_out1")]
        qk_rows = qk_dram.rearrange("(k p) c -> p k c", p=P)
        v_rows = v_dram.rearrange("p (g c) -> p g c", g=HKV)
        with nc.Block() as block:

            @block.sync
            def _(sp):
                for j in range(2):
                    sp.dma_start(h[:, j, :], h_dram[j * P:(j + 1) * P, :]).then_inc(h_in[j], 16)
                sp.dma_start(ident[:, :], const["ident"]).then_inc(const_in, 16)
                sp.dma_start(rope[:, :], const["rope"]).then_inc(const_in, 16)
                for k in range(KD):
                    sp.dma_start(w[:, k, :], w_dram[k * P:(k + 1) * P, :]).then_inc(w_in[k], 16)

                def load(j, par):
                    wait_alone(sp, hn_ready, j + 1, const_in, 32)
                    h_at = j * P + 2 * P
                    sp.dma_start(h[:, par, :], h_dram[ds(h_at, P), :]).then_inc(h_in[par], 16)

                def store_v(j, par):
                    wait_alone(sp, v_ready, j + 1, const_in, 32)
                    v_at = j * DH
                    sp.dma_start(v_rows[:, :, ds(v_at, DH)],
                                 v[:, par, :].rearrange("p (g c) -> p g c", g=HKV)).then_inc(v_out[par], 16)

                def store_qk(j, par):
                    wait_alone(sp, qkT_ready, j * NQ + NQ, const_in, 32)
                    qk_at = j * P
                    sp.dma_start(qk_rows[:, :, ds(qk_at, P)],
                                 qkT[:, par, :].rearrange("p (k c) -> p k c", k=SPLITS * NQK)).then_inc(qk_out[par], 16)

                def step(j, par):
                    load(j, par)
                    store_v(j, par)
                    if not (isinstance(j, int) and j == 0):
                        store_qk(j - 1, 1 - par)

                step(0, 0)
                step(1, 1)
                with sp.Fori(0, NT // 2 - 2) as r:
                    for c in (2, 3):
                        step(r * 2 + c, c % 2)
                for j in (NT - 2, NT - 1):
                    store_v(j, j % 2)
                    store_qk(j - 1, 1 - j % 2)
                store_qk(NT - 1, 1)
                for s in (*qk_out, *v_out):
                    sp.wait_ge(s, 16 * (NT // 2))

            @block.tensor
            def _(pe):
                def row_transposes(j, par):
                    pe.wait_ge(hn_ready, j + 1)
                    if not (isinstance(j, int) and j == 0):
                        pe.wait_ge(hT_ready, j)
                    for k in range(KD):
                        m = nc.tensor.transpose(ps_h[:, k * P:(k + 1) * P], hn[:, par, k * P:(k + 1) * P], ident[:, :])
                    m.then_inc(hT_done, 1)

                def qkv(j, par, n):
                    if n == 0:
                        pe.wait_ge(hT_ready, j + 1)
                    if not (isinstance(j, int) and j == 0):
                        pe.wait_ge(rope_done, j * 3 + (n - 2))
                        if n == 2:
                            pe.wait_ge(v_ready, j)
                    for k in range(KD):
                        if isinstance(j, int) and j == 0 and n == 0:
                            pe.wait_ge(w_in[k], 16 * use)
                        m = nc.tensor.matmul(ps_qkv[:, n * BANK:(n + 1) * BANK], hT[:, par, k * P:(k + 1) * P],
                                             w[:, k, n * BANK:(n + 1) * BANK], start=(k == 0), stop=(k == KD - 1))
                    m.then_inc(qkv_done, 1)

                def qk_transposes(j, par):
                    pe.wait_ge(parts_ready, j + 1)
                    if not (isinstance(j, int) and j == 0):
                        pe.wait_ge(qkT_ready, j * NQ)
                    for t, (a, n) in enumerate(TURNS):
                        if t >= 3:
                            pe.wait_ge(qkT_ready, j * NQ + (t - 2))
                        for c in range(0, n, P):
                            m = nc.tensor.transpose(ps_qk[:, t % 3, c:c + P], part[:, par, a + c:a + c + P],
                                                    ident_b[:, :])
                        m.then_inc(qkT_done, 1)

                def step(j, par, first, last):
                    qkv(j, par, 0)
                    qkv(j, par, 1)
                    if not last:
                        row_transposes(j + 1, 1 - par)
                    qkv(j, par, 2)
                    if not first:
                        qk_transposes(j - 1, 1 - par)

                pe.wait_ge(const_in, 32)
                pe.wait_ge(const_ready, 1)
                row_transposes(0, 0)
                over_tiles(pe, step)
                qk_transposes(NT - 1, (NT - 1) % 2)

            @block.scalar
            def _(act):
                def row_evac(j, par):
                    act.wait_ge(hT_done, j + 1)
                    if not (isinstance(j, int) and j < 2):
                        act.wait_ge(qkv_done, j * 3 - 3)
                    for a, n in chunks(D):
                        m = nc.scalar.copy(hT[:, par, a:a + n], ps_h[:, a:a + n])
                    m.then_inc(hT_ready, 1)

                def qk_evac(j, par):
                    for t, (a, n) in enumerate(TURNS):
                        act.wait_ge(qkT_done, j * NQ + (t + 1))
                        nc.scalar.copy(qkT[:, par, a:a + n], ps_qk[:, t % 3, 0:n]).then_inc(qkT_ready, 1)

                def step(j, par, first, last):
                    if not last:
                        row_evac(j + 1, 1 - par)
                    if not first:
                        if not (isinstance(j, int) and j < 3):
                            stored(j - 1, 1 - par, qk_out)
                        qk_evac(j - 1, 1 - par)

                def stored(j, par, sems):
                    act.wait_ge(sems[par], (j - par) * 8)

                row_evac(0, 0)
                step(0, 0, True, False)
                step(1, 1, False, False)
                step(2, 0, False, False)
                with act.Fori(0, (NT - 4) // 2) as r:
                    for c in (3, 4):
                        step(r * 2 + c, c % 2, False, False)
                step(NT - 1, (NT - 1) % 2, False, True)
                stored(NT - 1, (NT - 1) % 2, qk_out)
                qk_evac(NT - 1, (NT - 1) % 2)

            @block.gpsimd
            def _(pool):
                def step(j, par, first, last):
                    x = rot[:, par, :]
                    hi, mid, lo = (part[:, par, k * QK:(k + 1) * QK] for k in range(SPLITS))
                    if not (isinstance(j, int) and j < 2):
                        pool.wait_ge(qkT_done, j * NQ - NQ)
                    wait_alone(pool, rope_done, j * 3 + 3, const_in, 32)
                    nc.gpsimd.tensor_copy(hi, x)
                    pool.drain()
                    nc.gpsimd.tensor_tensor(x, x, hi, ALU.subtract)
                    pool.drain()
                    nc.gpsimd.tensor_copy(mid, x)
                    pool.drain()
                    nc.gpsimd.tensor_tensor(lo, x, mid, ALU.subtract).then_inc(parts_ready, 1)

                step(0, 0, True, False)
                step(1, 1, False, False)
                with pool.Fori(0, (NT - 4) // 2) as r:
                    for c in (2, 3):
                        step(r * 2 + c, c % 2, False, False)
                step(NT - 2, 0, False, False)
                step(NT - 1, 1, False, True)

            @block.vector
            def _(dve):
                def norm(j, par):
                    if isinstance(j, int):
                        dve.wait_ge(h_in[par], 16 * (j // 2 + 1))
                    else:
                        dve.wait_ge(h_in[par], (j - par) * 8 + 16)
                    if not (isinstance(j, int) and j < 2):
                        dve.wait_ge(hT_done, j - 1)
                    layer_norm(nc, dve, h[:, par, :], stats[:, par, :], mv[:, par, :], rstd[:, par, :],
                               hn[:, par, :]).then_inc(hn_ready, 1)

                def rotate(j, par, n):
                    heads = (BANK if n < 2 else QK - 2 * BANK) // DH
                    a, e = n * BANK, n * BANK + heads * DH
                    dve.wait_ge(qkv_done, j * 3 + n + 1)
                    if n == 0 and not (isinstance(j, int) and j < 2):
                        dve.wait_ge(parts_ready, j - 1)
                    x = ps_qkv[:, a:e].rearrange("p (h c) -> p h c", c=DH)
                    y = rot[:, par, a:e].rearrange("p (h c) -> p h c", c=DH)
                    z = half[:, n, 0:e - a].rearrange("p (h c) -> p h c", c=DH)
                    pos = (j % TT) * (2 * DH)

                    def table(at, size):
                        return rope[:, ds(pos + at, size)].unsqueeze(1).to_broadcast([P, heads, size])

                    nc.vector.tensor_tensor(y, x, table(0, DH), ALU.mult)
                    nc.vector.tensor_tensor(z[:, :, 0:HALF], x[:, :, HALF:DH], table(DH, HALF), ALU.mult)
                    nc.vector.tensor_tensor(z[:, :, HALF:DH], x[:, :, 0:HALF], table(DH + HALF, HALF), ALU.mult)
                    dve.drain()
                    nc.vector.tensor_tensor(rot[:, par, a:e], rot[:, par, a:e], half[:, n, 0:e - a],
                                            ALU.add).then_inc(rope_done, 1)

                def step(j, par, first, last):
                    if not last:
                        norm(j + 1, 1 - par)
                    for n in range(3):
                        rotate(j, par, n)
                    if not (isinstance(j, int) and j < 2):
                        dve.wait_ge(v_out[par], (j - par) * 8)
                    nc.vector.tensor_copy(v[:, par, :], ps_qkv[:, QK:QKV]).then_inc(v_ready, 1)

                dve.wait_ge(const_in, 32)
                nc.vector.tensor_copy(ident_b[:, :], ident[:, :]).then_inc(const_ready, 1)
                norm(0, 0)
                step(0, 0, True, False)
                step(1, 1, False, False)
                step(2, 0, False, False)
                with dve.Fori(0, (NT - 4) // 2) as r:
                    for c in (3, 4):
                        step(r * 2 + c, c % 2, False, False)
                step(NT - 1, (NT - 1) % 2, False, True)


def load_queries_keys(sp, gi, q, k, qk_dram, arrived, wait=None):
    g, b = gi % HKV, gi // HKV
    q_at, k_at, t_at = g * P, g * DH + H * DH, b * T
    if wait is not None:
        wait()
    for x in range(2):
        for r in range(4):
            rows = slice(r * DH, (r + 1) * DH)
            sp.dma_start(q[rows, x, :, :], qk_dram[ds(q_at + Q_PARTS[x][r] * QK, P), ds(t_at, T)].rearrange(
                "(m d) t -> d m t", d=DH)).then_inc(arrived, 16)
            sp.dma_start(k[rows, x, :], qk_dram[ds(k_at + K_PARTS[x][r] * QK, DH), ds(t_at, T)]).then_inc(arrived, 16)


def load_values(sp, gi, v, v_dram, arrived, wait=None):
    g, b = gi % HKV, gi // HKV
    v_at = g * (NT * DH) + b * (TT * DH)
    if wait is not None:
        wait()
    sp.dma_start(v, v_dram[:, ds(v_at, TT * DH)]).then_inc(arrived, 16)


def store_outputs(sp, gi, o, o_dram, done, wait):
    g, b = gi % HKV, gi // HKV
    j_at, c_at = b * TT, g * P
    wait()
    sp.dma_start(o_dram.rearrange("(j p) c -> p j c", p=P)[:, ds(j_at, TT), ds(c_at, P)], o).then_inc(done, 16)


def attention(nc, const, qk_dram, v_dram, o_dram):
    GROUPS = B * HKV
    STEPS = 2 * G * TT
    CHUNKS = [c for i in range(TT) for c in [(i, a) for a, _ in chunks((i + 1) * P)]]
    NC = len(CHUNKS)
    with ExitStack() as ctx:
        sb = lambda n, s, d=F32: ctx.enter_context(nc.sbuf_tensor("a0_" + n, s, d))
        ps = lambda n, s: ctx.enter_context(nc.psum_tensor("a0_" + n, s, F32))
        sem = lambda n: ctx.enter_context(nc.semaphore("a0_" + n))
        ident, bias_f = sb("ident", [P, P]), sb("bias_f", [P, P])
        ident_b, bias_b = sb("ident_b", [P, P], BF16), sb("bias_b", [P, P], BF16)
        q, k = sb("q", [P, 2, 2, G, T], BF16), sb("k", [P, 2, 2, T], BF16)
        v = sb("v", [P, 2, TT * DH])
        prob, probT = sb("prob", [P, 2, T]), sb("probT", [P, 2, T])
        top, shift, total = sb("top", [P, 2 * TT]), sb("shift", [P, 2 * TT]), sb("total", [P, 2, TT])
        inv = sb("inv", [P, 2, TT])
        o = sb("o", [P, 2, TT, G * DH])
        ps_s, ps_t, ps_o = ps("ps_s", [P, 2, 2 * BANK]), ps("ps_t", [P, 2, BANK]), ps("ps_o", [P, 2, BANK])
        const_in, const_ready = sem("const_in"), sem("const_ready")
        group_in = [sem("group_in0"), sem("group_in1")]
        s_done, shift_ready, exp_done, t_done = sem("s_done"), sem("shift_ready"), sem("exp_done"), sem("t_done")
        probT_act, probT_dve, pv_done, o_ready = sem("probT_act"), sem("probT_dve"), sem("pv_done"), sem("o_ready")
        o_out = [sem("o_out0"), sem("o_out1")]
        LOADED = 16 * 17

        def steps():
            n = 0
            for s in range(STEPS):
                i = s % TT
                mine = []
                for a, w in chunks((i + 1) * P):
                    mine.append((n, a, w))
                    n += 1
                yield s, s // TT, i, mine

        PLAN = list(steps())
        IC = 2 * G * NC

        with nc.Block() as block:

            @block.sync
            def _(sp):
                sp.dma_start(ident[:, :], const["ident"]).then_inc(const_in, 16)
                sp.dma_start(bias_f[:, :], const["causal"]).then_inc(const_in, 16)
                for x in range(2):
                    load_queries_keys(sp, x, q[:, x, :, :, :], k[:, x, :, :], qk_dram, group_in[x])
                    load_values(sp, x, v[:, x, :], v_dram, group_in[x])

                def store(gi, x, it):
                    store_outputs(sp, gi, o[:, x, :, :], o_dram, o_out[x],
                                  lambda: wait_alone(sp, o_ready, it * 2 * G + (x + 1) * G, const_in, 32))

                with sp.Fori(0, GROUPS // 2 - 1) as it:
                    for x in range(2):
                        store(it * 2 + x, x, it)
                        load_queries_keys(sp, it * 2 + (2 + x), q[:, x, :, :, :], k[:, x, :, :], qk_dram, group_in[x],
                                          lambda: wait_alone(sp, o_out[x], it * 16 + 16, const_in, 32))
                        load_values(sp, it * 2 + (2 + x), v[:, x, :], v_dram, group_in[x])
                for x in range(2):
                    store(GROUPS - 2 + x, x, GROUPS // 2 - 1)
                for x in range(2):
                    sp.wait_ge(o_out[x], 16 * (GROUPS // 2))

            @block.tensor
            def _(pe):
                pe.wait_ge(const_ready, 1)
                with pe.Fori(0, GROUPS // 2) as it:
                    def scores(s, unit, i, mine):
                        x, m = unit // G, unit % G
                        if unit % G == 0 and i == 0:
                            pe.wait_ge(group_in[x], it * LOADED + LOADED)
                        if s >= 2:
                            pe.wait_ge(exp_done, it * STEPS + (s - 1))
                        for a, w in chunks((i + 1) * P):
                            for y in range(2):
                                nc.tensor.matmul(ps_s[:, s % 2, a:a + w], q[:, x, y, m, i * P:(i + 1) * P],
                                                 k[:, x, y, a:a + w], start=(y == 0), stop=False,
                                                 skip_group_check=True)
                        nc.tensor.matmul(ps_s[:, s % 2, i * P:(i + 1) * P], ident_b[:, :], bias_b[:, :], start=False,
                                         stop=True, skip_group_check=True).then_inc(s_done, 1)

                    def evacuated(n):
                        if n % 2 == 0:
                            pe.wait_ge(probT_act, it * (IC // 2) + (n // 2 + 1))
                        else:
                            pe.wait_ge(probT_dve, it * (IC // 2) + (n // 2 + 1))

                    def turn(s, unit, i, mine):
                        pe.wait_ge(exp_done, it * STEPS + (s + 1))
                        for n, a, w in mine:
                            if n >= 2:
                                evacuated(n - 2)
                            for c in range(0, w, P):
                                mm = nc.tensor.transpose(ps_t[:, n % 2, c:c + P], prob[:, s % 2, a + c:a + c + P],
                                                         ident[:, :])
                            mm.then_inc(t_done, 1)

                    def values(s, unit, i, mine):
                        if unit >= 2 and i == 0:
                            pe.wait_ge(o_ready, it * (2 * G) + (unit - 1))
                        for n, a, w in mine:
                            evacuated(n)
                        x = unit // G
                        for b in range(i + 1):
                            mm = nc.tensor.matmul(ps_o[:, unit % 2, i * DH:(i + 1) * DH], probT[:, s % 2, b * P:(b + 1) * P],
                                                  v[:, x, b * DH:(b + 1) * DH], start=(b == 0), stop=(b == i))
                        mm.then_inc(pv_done, 1)

                    scores(*PLAN[0])
                    scores(*PLAN[1])
                    for s in range(STEPS):
                        turn(*PLAN[s])
                        if s + 2 < STEPS:
                            scores(*PLAN[s + 2])
                        if s >= 1:
                            values(*PLAN[s - 1])
                    values(*PLAN[STEPS - 1])

            @block.scalar
            def _(act):
                with act.Fori(0, GROUPS // 2) as it:
                    def exps(s, unit, i, mine):
                        act.wait_ge(shift_ready, it * STEPS + (s + 1))
                        if s >= 2:
                            act.wait_ge(t_done, it * IC + PLAN[s - 2][3][-1][0] + 1)
                        w = (i + 1) * P
                        nc.scalar.activation(prob[:, s % 2, 0:w], ps_s[:, s % 2, 0:w], ACT.Exp, scale=SCALE,
                                             bias=shift[:, s % 16:s % 16 + 1],
                                             accum_out=total[:, unit % 2, i:i + 1]).then_inc(exp_done, 1)

                    def evac(s, unit, i, mine):
                        for n, a, w in mine:
                            if n % 2 == 0:
                                act.wait_ge(t_done, it * IC + n + 1)
                                nc.scalar.copy(probT[:, s % 2, a:a + w], ps_t[:, n % 2, 0:w]).then_inc(probT_act, 1)

                    exps(*PLAN[0])
                    for s in range(STEPS):
                        if s + 1 < STEPS:
                            exps(*PLAN[s + 1])
                        evac(*PLAN[s])

            @block.vector
            def _(dve):
                dve.wait_ge(const_in, 32)
                nc.vector.tensor_copy(ident_b[:, :], ident[:, :])
                nc.vector.tensor_copy(bias_b[:, :], bias_f[:, :]).then_inc(const_ready, 1)
                with dve.Fori(0, GROUPS // 2) as it:
                    def maxima(s, unit, i, mine):
                        dve.wait_ge(s_done, it * STEPS + (s + 1))
                        c = s % 16
                        nc.vector.tensor_reduce(top[:, c:c + 1], ps_s[:, s % 2, 0:(i + 1) * P], AX_X, ALU.max)
                        dve.drain()
                        nc.vector.tensor_scalar(shift[:, c:c + 1], top[:, c:c + 1], -SCALE, None,
                                                ALU.mult).then_inc(shift_ready, 1)

                    def evac(s, unit, i, mine):
                        for n, a, w in mine:
                            if n % 2 == 1:
                                dve.wait_ge(t_done, it * IC + n + 1)
                                nc.vector.tensor_copy(probT[:, s % 2, a:a + w],
                                                      ps_t[:, n % 2, 0:w]).then_inc(probT_dve, 1)

                    def normalise(unit):
                        x, m = unit // G, unit % G
                        dve.wait_ge(pv_done, it * STEPS + (unit + 1) * TT)
                        nc.vector.reciprocal(inv[:, unit % 2, :], total[:, unit % 2, :])
                        dve.drain()
                        nc.vector.tensor_tensor(o[:, x, :, m * DH:(m + 1) * DH],
                                                ps_o[:, unit % 2, 0:TT * DH].rearrange("p (i c) -> p i c", c=DH),
                                                inv[:, unit % 2, :].unsqueeze(2).to_broadcast([P, TT, DH]),
                                                ALU.mult).then_inc(o_ready, 1)

                    maxima(*PLAN[0])
                    for s in range(STEPS):
                        if s + 1 < STEPS:
                            maxima(*PLAN[s + 1])
                        evac(*PLAN[s])
                        if s % TT == 2 and s > TT:
                            normalise(s // TT - 1)
                    normalise(2 * G - 1)


def kept_attention(nc, const, qk_dram, v_dram, o_dram):
    PAIRS = B * H // 2
    PPG = G // 2
    TILES = [(m, i) for m in range(2) for i in range(TT)]
    RANKED = [(m, i) for m, i in TILES if i]
    CH = [(n, m, i, a, w) for n, (m, i, a, w) in enumerate(
        (m, i, a, w) for m, i in TILES for a, w in chunks((i + 1) * P))]
    NC = len(CH)
    with ExitStack() as ctx:
        sb = lambda n, s, d=F32: ctx.enter_context(nc.sbuf_tensor("a1_" + n, s, d))
        ps = lambda n, s: ctx.enter_context(nc.psum_tensor("a1_" + n, s, F32))
        sem = lambda n: ctx.enter_context(nc.semaphore("a1_" + n))
        ident, bias_f = sb("ident", [P, P]), sb("bias_f", [P, P])
        ident_b, bias_b = sb("ident_b", [P, P], BF16), sb("bias_b", [P, P], BF16)
        table = sb("table", [P, 5, NS])
        iota = sb("iota", [P, 8])
        q, k, v = sb("q", [P, 2, G, T], BF16), sb("k", [P, 2, T], BF16), sb("v", [P, TT * DH])
        x = sb("x", [P, 2, 2 * SEG])
        prob = sb("prob", [P, 2, 2 * SEG])
        probT = sb("probT", [P, 2, T])
        o = sb("o", [P, TT, G * DH])
        sign = sb("sign", [P, SEG], BF16)
        above = sb("above", [P, 2, T], BF16)
        below = sb("below", [P, 2, T])
        top, shift = sb("top", [P, 2, 2 * TT]), sb("shift", [P, 2, 2 * TT])
        total, inv = sb("total", [P, 2, 2 * TT]), sb("inv", [P, 2 * TT])
        stats, mv = sb("stats", [P, NS, 6]), sb("mv", [P, NS, 2])
        var, var_h, tmp, rs, dev = (sb(n, [P, NS]) for n in ("var", "var_h", "tmp", "rs", "dev"))
        state = sb("state", [P, 2, 4, NS])
        bracket = sb("bracket", [P, 2, 2, 2, NS])
        side = sb("side", [P, 2, NS], I32)
        span, new, open_ = sb("span", [P, 2, NS]), sb("new", [P, NS]), sb("open", [P, NS], I32)
        miss, miss2 = sb("miss", [P, NS]), sb("miss2", [P, NS])
        exact = sb("exact", [P, NS])
        rank, nine = sb("rank", [P, NS]), sb("nine", [P, NS, 9])
        hot, pick = sb("hot", [P, NS, 8]), sb("pick", [P, NS, 8])
        limit, follow = sb("limit", [P, NS]), sb("follow", [P, NS])
        fail, failT = sb("fail", [P, 32]), sb("failT", [P, 32])
        fail2, fail2T, flag, any_flag = sb("fail2", [P, 32]), sb("fail2T", [P, 32]), sb("flag", [P, 32], I32), sb("any", [P, 1], I32)
        quadrants = sb("quadrants", [1, 4], I32)
        best, floor = sb("best", [P, 8]), sb("floor", [P, 1])
        ps_s, ps_t, ps_o = ps("ps_s", [P, 2, 2 * BANK]), ps("ps_t", [P, 3, BANK]), ps("ps_o", [P, 2 * TT, DH])
        const_in, const_ready = sem("const_in"), sem("const_ready")
        qk_in, v_in, o_out = sem("qk_in"), sem("v_in"), sem("o_out")
        s_done, x_ready = sem("s_done"), sem("x_ready")
        t_ready, signs_done = sem("t_ready"), sem("signs_done")
        exp_done, prob_ready = sem("exp_done"), sem("prob_ready")
        turn_done, probT_ready, pv_done, o_ready = sem("turn_done"), sem("probT_ready"), sem("pv_done"), sem("o_ready")

        def ps_seg(m, i):
            return m * SEG + off(i)

        def stages(s):
            return dict(score=s + 1 < PAIRS, search=0 <= s < PAIRS, keep=0 <= s - 1 < PAIRS, value=0 <= s - 2 < PAIRS)

        ALL = dict(score=True, search=True, keep=True, value=True)
        FIRST_LOOP, LOOPS = 4, (PAIRS - 6) // 2

        def over_slots(eng, slot):
            for s in range(-1, FIRST_LOOP):
                slot(s, s % 2, stages(s))
            with eng.Fori(0, LOOPS) as r:
                for c in (0, 1):
                    slot(r * 2 + (FIRST_LOOP + c), c, ALL)
            for s in range(FIRST_LOOP + 2 * LOOPS, PAIRS + 2):
                slot(s, s % 2, stages(s))

        def share(seq, part, parts):
            return seq[len(seq) * part // parts:len(seq) * (part + 1) // parts]

        with nc.Block() as block:

            @block.sync
            def _(sp):
                sp.dma_start(ident[:, :], const["ident"]).then_inc(const_in, 16)
                sp.dma_start(bias_f[:, :], const["causal"]).then_inc(const_in, 16)
                sp.dma_start(table[:, :, :], const["search"].rearrange("p (a n) -> p a n", a=5)).then_inc(const_in, 16)
                sp.dma_start(iota[:, :], const["iota"][:, 0:8]).then_inc(const_in, 16)
                load_queries_keys(sp, 0, q[:, :, :, :], k[:, :, :], qk_dram, qk_in)
                load_values(sp, 0, v[:, :], v_dram, v_in)

                def load_next(g):
                    load_queries_keys(sp, g + 1, q[:, :, :, :], k[:, :, :], qk_dram, qk_in,
                                      lambda: wait_alone(sp, s_done, g * (4 * TT) + 4 * TT, const_in, 64))

                def group(g, ahead, more):
                    if ahead:
                        load_next(g + 1)
                    store_outputs(sp, g, o[:, :, :], o_dram, o_out,
                                  lambda: wait_alone(sp, o_ready, g * PPG + PPG, const_in, 64))
                    wait_alone(sp, o_out, g * 16 + 16, const_in, 64)
                    if more:
                        load_values(sp, g + 1, v[:, :], v_dram, v_in)

                load_next(0)
                with sp.Fori(0, B * HKV - 2) as g:
                    group(g, True, True)
                group(B * HKV - 2, False, True)
                group(B * HKV - 1, False, False)

            @block.tensor
            def _(pe):
                pe.wait_ge(const_ready, 1)

                def slot(s, par, st):
                    def scores(n):
                        m, i = TILES[n]
                        if n == 0 and (1 - par) == 0:
                            pe.wait_ge(qk_in, (s + 1) * 128 + 256)
                        if not (isinstance(s, int) and s < 0 and n < 2):
                            pe.wait_ge(x_ready, (s + 1) * (2 * TT) + (n - 1))
                        head = ((1 - par) * 2) + m
                        for a, w in chunks((i + 1) * P):
                            for y in range(2):
                                nc.tensor.matmul(ps_s[:, n % 2, a:a + w], q[:, y, head, i * P:(i + 1) * P],
                                                 k[:, y, a:a + w], start=(y == 0), stop=False,
                                                 skip_group_check=True)
                        nc.tensor.matmul(ps_s[:, n % 2, i * P:(i + 1) * P], ident_b[:, :], bias_b[:, :], start=False,
                                         stop=True, skip_group_check=True).then_inc(s_done, 1)

                    def turn(n, m, i, a, w):
                        if not (isinstance(s, int) and s == 2 and n < 3):
                            pe.wait_ge(probT_ready, (s - 2) * NC + (n - 2))
                        for c in range(0, w, P):
                            at = ps_seg(m, i) + a + c
                            mm = nc.tensor.transpose(ps_t[:, n % 3, c:c + P], prob[:, par, at:at + P], ident[:, :])
                        mm.then_inc(turn_done, 1)

                    def values(n):
                        m, i = TILES[n]
                        last = [c for c in CH if c[1:3] == (m, i)][-1][0]
                        pe.wait_ge(probT_ready, (s - 2) * NC + (last + 1))
                        for b in range(i + 1):
                            mm = nc.tensor.matmul(ps_o[:, n, :], probT[:, n % 2, b * P:(b + 1) * P],
                                                  v[:, b * DH:(b + 1) * DH], start=(b == 0), stop=(b == i))
                        mm.then_inc(pv_done, 1)

                    if st["value"]:
                        if par == 0:
                            pe.wait_ge(v_in, (s - 2) * 8 + 16)
                        pe.wait_ge(prob_ready, (s - 2) * NS + NS)
                        if not (isinstance(s, int) and s == 2):
                            pe.wait_ge(o_ready, s - 2)
                        for n in range(2 * TT):
                            for c in CH:
                                if c[1:3] == TILES[n]:
                                    turn(*c)
                            if n:
                                values(n - 1)
                        values(2 * TT - 1)
                    if st["score"]:
                        for n in range(2 * TT):
                            scores(n)

                over_slots(pe, slot)

            @block.scalar
            def _(act):
                def slot(s, par, st):
                    def evac(n, m, i, a, w):
                        tile = TILES.index((m, i))
                        act.wait_ge(turn_done, (s - 2) * NC + (n + 1))
                        nc.scalar.copy(probT[:, tile % 2, a:a + w], ps_t[:, n % 3, 0:w]).then_inc(probT_ready, 1)

                    EVAC_PASSES = 2
                    counted = [sum(2 + i for _, i in (RANKED * EVAC_PASSES)[:k]) for k in range(EVAC_PASSES * NS + 1)]
                    moved = [sum(c[4] for c in CH[:k]) for k in range(NC)]
                    after = [sum(f * moved[-1] < g * counted[-1] for f in counted[1:]) for g in moved]

                    def evacs(step):
                        if st["value"]:
                            for k, c in enumerate(CH):
                                if min(after[k], EVAC_PASSES * NS - 1) == step:
                                    evac(*c)

                    def count(p):
                        if p == 0:
                            act.drain()
                        act.wait_ge(t_ready, s * PASSES + (p + 1))
                        for n, (m, i) in enumerate(RANKED):
                            at, w = ps_seg(m, i), (i + 1) * P
                            if n == TT - 1:
                                act.drain()
                            ins = nc.scalar.activation(sign[:, off(i):off(i) + w], x[:, par, at:at + w], ACT.Sign, scale=-1.0,
                                                       bias=state[:, par, 0, n:n + 1], accum_out=state[:, par, 2, n:n + 1])
                            if n < NS - 1:
                                evacs(p * NS + n)
                        ins.then_inc(signs_done, 1)
                        evacs(p * NS + NS - 1)

                    def exps(n, y):
                        m, i = TILES[n]
                        at, w = ps_seg(m, i), (i + 1) * P
                        if i:
                            ins = nc.scalar.activation(prob[:, y, at:at + w], x[:, y, at:at + w], ACT.Exp, scale=SCALE,
                                                       bias=shift[:, y, n:n + 1])
                        else:
                            ins = nc.scalar.activation(prob[:, y, at:at + w], x[:, y, at:at + w], ACT.Exp, scale=SCALE,
                                                       bias=shift[:, y, n:n + 1], accum_out=total[:, y, n:n + 1])
                        ins.then_inc(exp_done, 1)

                    EXPS = {2: range(0, TT + 3), 3: range(TT + 3, 2 * TT)}
                    for p in range(PASSES):
                        if st["search"]:
                            count(p)
                        else:
                            for n in range(NS):
                                evacs(p * NS + n)
                        if st["search"] and p in EXPS:
                            if p == 2 and not (isinstance(s, int) and s < 2):
                                act.wait_ge(o_ready, s - 1)
                            for n in EXPS[p]:
                                exps(n, par)

                over_slots(act, slot)

            @block.vector
            def _(dve):
                dve.wait_ge(const_in, 64)
                nc.vector.tensor_copy(ident_b[:, :], ident[:, :])
                nc.vector.tensor_copy(bias_b[:, :], bias_f[:, :]).then_inc(const_ready, 1)
                nc.vector.memset(fail[:, :], 0.0)
                nc.vector.memset(fail2[:, :], 0.0)
                nc.vector.memset(floor[:, :], MASKED)
                dve.drain()
                quantile, per_sign, aim, sign_low, sign_high = (table[:, k_, :] for k_ in range(5))
                for z in range(2):
                    for c in (1, 3):
                        nc.vector.tensor_copy(state[:, z, c, :], aim)

                def slot(s, par, st):
                    y = 1 - par
                    t, signs = state[:, par, 0, :], state[:, par, 2, :]

                    def start(z):
                        t0 = state[:, z, 0, :]
                        dve.drain()
                        for n, (m, i) in enumerate(RANKED):
                            at = ps_seg(m, i)
                            step = 1 if i == 1 else 2 if i < 4 else 4
                            nc.vector.bn_stats(stats[:, n, :], x[:, z, at:at + i * P:step])
                        nc.vector.tensor_scalar(shift[:, z, :], top[:, z, :], -SCALE, None, ALU.mult)
                        dve.drain()
                        for n in range(NS):
                            nc.vector.bn_aggr(mv[:, n, :], stats[:, n, :])
                        dve.drain()
                        nc.vector.tensor_scalar(var[:, :], mv[:, :, 1], 1e-20, None, ALU.add)
                        nc.vector.tensor_scalar(var_h[:, :], mv[:, :, 1], 1e-20, -0.5, ALU.add, ALU.mult)
                        dve.drain()
                        inv_sqrt(nc, dve, var[:, :], var_h[:, :], tmp[:, :], rs[:, :], 1)
                        nc.vector.tensor_tensor(dev[:, :], var[:, :], rs[:, :], ALU.mult)
                        dve.drain()
                        nc.vector.tensor_tensor(tmp[:, :], dev[:, :], quantile, ALU.mult)
                        nc.vector.scalar_tensor_tensor(out=bracket[:, z, 0, 0, :], in0=dev[:, :], scalar=-2.5,
                                                       in1=mv[:, :, 0], op0=ALU.mult, op1=ALU.add)
                        nc.vector.tensor_copy(bracket[:, z, 0, 1, :], sign_low)
                        for m in range(2):
                            nc.vector.tensor_copy(bracket[:, z, 1, 0, m * (TT - 1):(m + 1) * (TT - 1)],
                                                  top[:, z, m * TT + 1:(m + 1) * TT])
                        nc.vector.tensor_copy(bracket[:, z, 1, 1, :], sign_high)
                        dve.drain()
                        nc.vector.tensor_tensor(tmp[:, :], tmp[:, :], mv[:, :, 0], ALU.add)
                        nc.vector.tensor_tensor(dev[:, :], dev[:, :], per_sign, ALU.mult)
                        dve.drain()
                        nc.vector.tensor_tensor(t0, tmp[:, :], bracket[:, z, 1, 0, :], ALU.min).then_inc(t_ready, 1)

                    def narrow(p):
                        low, span_t, span_s = bracket[:, par, 0, :, :], span[:, 0, :], span[:, 1, :]
                        dve.wait_ge(signs_done, s * PASSES + (p + 1))
                        nc.vector.tensor_tensor(side[:, :, :], state[:, par, 2:4, :], state[:, par, 1:3, :], ALU.is_lt)
                        nc.vector.tensor_tensor(miss[:, :], signs, aim, ALU.subtract)
                        dve.drain()
                        nc.vector.copy_predicated(bracket[:, par, :, 0, :], side[:, :, :],
                                                  t.unsqueeze(1).to_broadcast([P, 2, NS]))
                        nc.vector.copy_predicated(bracket[:, par, :, 1, :], side[:, :, :],
                                                  signs.unsqueeze(1).to_broadcast([P, 2, NS]))
                        nc.vector.tensor_tensor(miss2[:, :], miss[:, :], miss[:, :], ALU.mult)
                        if p == 0:
                            nc.vector.tensor_tensor(new[:, :], miss[:, :], dev[:, :], ALU.mult)
                            dve.drain()
                            nc.vector.tensor_scalar(open_[:, :], miss2[:, :], 7.2 ** 2, None, ALU.is_gt)
                            nc.vector.tensor_tensor(new[:, :], new[:, :], t, ALU.add)
                            dve.drain()
                            nc.vector.tensor_tensor(new[:, :], new[:, :], bracket[:, par, 1, 0, :], ALU.min)
                            dve.drain()
                            nc.vector.tensor_tensor(new[:, :], new[:, :], low[:, 0, :], ALU.max)
                        else:
                            dve.drain()
                            nc.vector.tensor_tensor(span[:, :, :], low, bracket[:, par, 1, :, :], ALU.subtract)
                            nc.vector.tensor_tensor(new[:, :], low[:, 1, :], aim, ALU.subtract)
                            nc.vector.tensor_scalar(open_[:, :], miss2[:, :], 7.2 ** 2, None, ALU.is_gt)
                            dve.drain()
                            nc.vector.reciprocal(rs[:, :], span_s)
                            nc.vector.tensor_tensor(new[:, :], new[:, :], span_t, ALU.mult)
                            dve.drain()
                            nc.vector.tensor_tensor(new[:, :], new[:, :], rs[:, :], ALU.mult)
                            dve.drain()
                            nc.vector.tensor_tensor(new[:, :], low[:, 0, :], new[:, :], ALU.subtract)
                        dve.drain()
                        ins = nc.vector.copy_predicated(t, open_[:, :], new[:, :])
                        if p < PASSES - 1:
                            ins.then_inc(t_ready, 1)

                    def rank_steps(n, r):
                        m, i = RANKED[n]
                        at, w = ps_seg(m, i), (i + 1) * P
                        tl = state[:, y, 0, n:n + 1]
                        return (
                            lambda: nc.vector.tensor_scalar(above[:, r, 0:w], x[:, y, at:at + w], tl, None, ALU.is_ge,
                                                            ALU.add, accum_out=exact[:, n:n + 1]),
                            lambda: nc.vector.scalar_tensor_tensor(out=below[:, r, 0:w], in0=above[:, r, 0:w],
                                                                   scalar=MASKED, in1=x[:, y, at:at + w], op0=ALU.mult,
                                                                   op1=ALU.add),
                            lambda: nc.vector.max(nine[:, n, 1:9], below[:, r, 0:w]),
                        )

                    def rank_some(mine):
                        todo = [rank_steps(n, k % 2) for k, n in enumerate(mine)]
                        for c in range(len(mine) + 2 if todo else 0):
                            for d in (2, 1, 0):
                                if 0 <= c - d < len(mine):
                                    todo[c - d][d]()
                            dve.drain()

                    def choose():
                        tl = state[:, y, 0, :]
                        nc.vector.tensor_scalar(rank[:, :], exact[:, :], -1.0, float(KEEP), ALU.mult, ALU.add)
                        nc.vector.tensor_copy(nine[:, :, 0], tl)
                        dve.drain()
                        nc.vector.tensor_tensor(hot[:, :, :], iota[:, :].unsqueeze(1).to_broadcast([P, NS, 8]),
                                                rank[:, :].unsqueeze(2).to_broadcast([P, NS, 8]), ALU.is_equal)
                        dve.drain()
                        nc.vector.tensor_tensor(pick[:, :, :], hot[:, :, :], nine[:, :, 0:8], ALU.mult)
                        dve.drain()
                        nc.vector.tensor_reduce(limit[:, :], pick[:, :, :], AX_X, ALU.add)
                        nc.vector.tensor_tensor(hot[:, :, :], hot[:, :, :], nine[:, :, 1:9], ALU.mult)
                        dve.drain()
                        nc.vector.tensor_reduce(follow[:, :], hot[:, :, :], AX_X, ALU.add)
                        dve.drain()
                        nc.vector.tensor_tensor(fail[:, 0:NS], follow[:, :], limit[:, :], ALU.is_lt)
                        dve.drain()
                        nc.vector.tensor_scalar(fail[:, 0:NS], fail[:, 0:NS], -1.0, 1.0, ALU.mult, ALU.add)
                        dve.drain()
                        nc.vector.transpose(failT[:, :], fail[:, :])
                        dve.drain()
                        nc.vector.tensor_reduce(fail2[:, 0:1], failT[:, :], AX_X, ALU.max)
                        dve.drain()
                        nc.vector.transpose(fail2T[:, :], fail2[:, :])
                        dve.drain()
                        nc.vector.tensor_copy(flag[:, :], fail2T[:, :])
                        nc.vector.tensor_reduce(any_flag[:, :], fail2T[:, :], AX_X, ALU.max)
                        dve.drain()

                    def raised(col):
                        for k in range(4):
                            nc.vector.tensor_copy(quadrants[:, k:k + 1], col[32 * k:32 * k + 1, :])
                        dve.drain()
                        nc.vector.tensor_reduce(any_flag[0:1, :], quadrants[:, :], AX_X, ALU.max)
                        dve.drain()
                        dve.reg_load(any_raised, any_flag[0:1, :])
                        return any_raised

                    def select_exactly(n):
                        m, i = RANKED[n]
                        at, w = ps_seg(m, i), (i + 1) * P
                        left, lost = below[:, 0, 0:w], below[:, 1, 0:w].bitcast(I32)
                        nc.vector.tensor_copy(left, x[:, y, at:at + w])
                        dve.drain()
                        with dve.Fori(0, KEEP // 8):
                            nc.vector.max(best[:, :], left)
                            dve.drain()
                            nc.vector.match_replace(out=left, in_to_replace=best[:, :], in_values=left,
                                                    imm_value=TAKEN)
                            dve.drain()
                        nc.vector.tensor_scalar(lost, left, TAKEN / 2, None, ALU.is_gt)
                        nc.vector.memset(limit[:, n:n + 1], MASKED / 2)
                        dve.drain()
                        nc.vector.copy_predicated(x[:, y, at:at + w], lost, floor[:, :].to_broadcast([P, w]))
                        dve.drain()

                    def keep(n):
                        m, i = TILES[n]
                        if i == 0:
                            return
                        r = RANKED.index((m, i))
                        at, w = ps_seg(m, i), (i + 1) * P
                        if n == 1:
                            dve.wait_ge(exp_done, (s - 1) * (2 * TT) + 2 * TT)
                        nc.vector.scalar_tensor_tensor(out=prob[:, y, at:at + w], in0=x[:, y, at:at + w],
                                                       scalar=limit[:, r:r + 1], in1=prob[:, y, at:at + w],
                                                       op0=ALU.is_ge, op1=ALU.mult,
                                                       accum_out=total[:, y, n:n + 1]).then_inc(prob_ready, 1)

                    def fetch(n):
                        m, i = TILES[n]
                        at, w = ps_seg(m, i), (i + 1) * P
                        dve.wait_ge(s_done, (s + 1) * (2 * TT) + (n + 1))
                        nc.vector.tensor_scalar(x[:, y, at:at + w], ps_s[:, n % 2, 0:w], 1.0, None, ALU.mult, ALU.max,
                                                accum_out=top[:, y, n:n + 1]).then_inc(x_ready, 1)

                    def keep_and_fetch(tiles):
                        for first in tiles[::2]:
                            if st["keep"]:
                                for n in (first, first + 1):
                                    keep(n)
                                dve.drain()
                            if st["score"]:
                                for n in (first, first + 1):
                                    fetch(n)

                    def normalise():
                        dve.wait_ge(pv_done, (s - 2) * (2 * TT) + 2 * TT)
                        nc.vector.reciprocal(inv[:, :], total[:, par, :])
                        dve.drain()
                        for m in range(2):
                            c = (2 * par + m) * DH
                            ins = nc.vector.tensor_tensor(
                                o[:, :, c:c + DH], ps_o[:, m * TT:(m + 1) * TT, :],
                                inv[:, m * TT:(m + 1) * TT].unsqueeze(2).to_broadcast([P, TT, DH]), ALU.mult)
                        ins.then_inc(o_ready, 1)

                    def exact_where_needed():
                        with dve.If_ne(raised(any_flag), 0):
                            wait_alone(dve, exp_done, (s - 1) * (2 * TT) + 2 * TT, const_in, 64)
                            for n in range(NS):
                                with dve.If_ne(raised(flag[:, n:n + 1]), 0):
                                    select_exactly(n)
                                dve.nop()
                        dve.nop()
                        dve.drain()

                    RANKS = [[*range(0, TT - 2), TT - 1], [TT - 2, *range(TT + 1, NS)], [TT], (), ()]
                    KEEPS = [(), (), range(0, 4), range(4, 14), range(14, 2 * TT)]

                    def part(p):
                        if st["keep"]:
                            rank_some(RANKS[p])
                            if p == 2:
                                choose()
                                exact_where_needed()
                        if p == 2 and st["value"]:
                            normalise()
                        keep_and_fetch(KEEPS[p])
                        if p == 4 and st["score"]:
                            start(y)

                    for p in range(PASSES):
                        part(p)
                        if st["search"]:
                            narrow(p)
                            dve.drain()

                any_raised = dve.alloc_register("any_raised")
                over_slots(dve, slot)


def mixture(nc, tag, w_in, use, wo_dram, ar_dram, b_dram, base_dram, bias_dram, const, h_dram, o_dram, out_dram):
    top2 = base_dram is not None
    AR = ER + NE
    with ExitStack() as ctx:
        sb = lambda n, s, d=F32: ctx.enter_context(nc.sbuf_tensor(tag + n, s, d))
        ps = lambda n, s: ctx.enter_context(nc.psum_tensor(tag + n, s, F32))
        sem = lambda n: ctx.enter_context(nc.semaphore(tag + n))
        ident = sb("ident", [P, P])
        iota = sb("iota", [P, NE])
        wo = sb("wo", [P, KD, D])
        base = sb("base", [P, KD, D]) if top2 else None
        ar = sb("ar", [P, KD, AR])
        bT = sb("bT", [P, D])
        bias = sb("bias", [P, D if top2 else NE])
        o, h, y = sb("o", [P, 2, D]), sb("h", [P, 2, D]), sb("y", [P, 2, D])
        hn = sb("hn", [P, D])
        oT, hT = sb("oT", [P, D]), sb("hT", [P, D])
        low, lowT = sb("low", [P, ER]), sb("lowT", [P, P])
        stats, mv, rstd = sb("stats", [P, 12]), sb("mv", [P, 2]), sb("rstd", [P, 4])
        logit, mix, one = sb("logit", [P, NE]), sb("mix", [P, NE]), sb("one", [P, NE])
        top, neg, total, inv = sb("top", [P, 1]), sb("neg", [P, 1]), sb("total", [P, 1]), sb("inv", [P, 1])
        weight = sb("weight", [P, NE])
        expd, best, at, at_f = sb("expd", [P, NE]), sb("best", [P, 8]), sb("at", [P, 8], U32), sb("at_f", [P, 2])
        part = sb("part", [P, 2])
        ps_wo, ps_y, ps_t = ps("ps_wo", [P, D]), ps("ps_y", [P, D]), ps("ps_t", [P, D])
        ps_a, ps_l = ps("ps_a", [P, BANK]), ps("ps_l", [P, BANK])
        const_in, rest_in = sem("const_in"), sem("rest_in")
        base_in = sem("base_in")
        o_in, h_in, y_out = [sem("o_in0"), sem("o_in1")], [sem("h_in0"), sem("h_in1")], [sem("y_out0"), sem("y_out1")]
        oT_done, oT_ready, wo_done, added = sem("oT_done"), sem("oT_ready"), sem("wo_done"), sem("added")
        hn_ready, hT_done, hT_ready, a_done = sem("hn_ready"), sem("hT_done"), sem("hT_ready"), sem("a_done")
        neg_ready, exp_done, low_ready = sem("neg_ready"), sem("exp_done"), sem("low_ready")
        lowT_done, lowT_ready, y_done, y_ready = sem("lowT_done"), sem("lowT_ready"), sem("y_done"), sem("y_ready")
        ab_loads = 4

        with nc.Block() as block:

            @block.sync
            def _(sp):
                for j in range(2):
                    sp.dma_start(o[:, j, :], o_dram[j * P:(j + 1) * P, :]).then_inc(o_in[j], 16)
                    sp.dma_start(h[:, j, :], h_dram[j * P:(j + 1) * P, :]).then_inc(h_in[j], 16)
                sp.dma_start(ident[:, :], const["ident"]).then_inc(const_in, 16)
                for k in range(KD):
                    sp.dma_start(wo[:, k, :], wo_dram[k * P:(k + 1) * P, :]).then_inc(w_in[k], 16)
                sp.dma_start(iota[:, :], const["iota"][:, 0:NE]).then_inc(rest_in, 16)
                sp.dma_start(bias[:, :], bias_dram.partition_broadcast(P)).then_inc(rest_in, 16)
                sp.dma_start(ar[:, :, :], ar_dram.rearrange("(k p) n -> p k n", p=P)).then_inc(rest_in, 16)
                sp.dma_start(bT[:, :], b_dram).then_inc(rest_in, 16)
                if top2:
                    sp.dma_start(base[:, :, :], base_dram.rearrange("(k p) n -> p k n", p=P)).then_inc(base_in, 16)

                def store(j, par, at):
                    wait_alone(sp, y_ready, j + 1, const_in, 16)
                    sp.dma_start(out_dram[ds(at, P), :],
                                 y[:, par, :]).then_inc(y_out[par], 16)

                def step(j, par):
                    next_at, at = j * P + 2 * P, j * P
                    wait_alone(sp, oT_done, j + 1, const_in, 16)
                    sp.dma_start(o[:, par, :], o_dram[ds(next_at, P), :]).then_inc(o_in[par], 16)
                    store(j, par, at)
                    sp.dma_start(h[:, par, :], h_dram[ds(next_at, P), :]).then_inc(h_in[par], 16)

                with sp.Fori(0, NT // 2 - 1) as r:
                    for c in (0, 1):
                        step(r * 2 + c, c)
                for c in (0, 1):
                    store(NT - 2 + c, c, (NT - 2 + c) * P)
                for c in (0, 1):
                    sp.wait_ge(y_out[c], 16 * (NT // 2))

            @block.tensor
            def _(pe):
                def out_transposes(j, par):
                    pe.wait_ge(o_in[par], (j - par) * 8 + 16)
                    if not (isinstance(j, int) and j == 0):
                        pe.wait_ge(hT_ready, j)
                    for k in range(KD):
                        m = nc.tensor.transpose(ps_t[:, k * P:(k + 1) * P], o[:, par, k * P:(k + 1) * P], ident[:, :])
                    m.then_inc(oT_done, 1)

                def out_project(j, par):
                    pe.wait_ge(oT_ready, j + 1)
                    if not (isinstance(j, int) and j == 0):
                        pe.wait_ge(added, j)
                    for a, n in chunks(D):
                        for k in range(KD):
                            if isinstance(j, int) and j == 0 and a == 0:
                                pe.wait_ge(w_in[k], 16 * use)
                            m = nc.tensor.matmul(ps_wo[:, a:a + n], oT[:, k * P:(k + 1) * P], wo[:, k, a:a + n],
                                                 start=(k == 0), stop=(k == KD - 1))
                        m.then_inc(wo_done, 1)

                def row_transposes(j, par):
                    pe.wait_ge(hn_ready, j + 1)
                    pe.wait_ge(oT_ready, j + 1)
                    for k in range(KD):
                        m = nc.tensor.transpose(ps_t[:, k * P:(k + 1) * P], hn[:, k * P:(k + 1) * P], ident[:, :])
                    m.then_inc(hT_done, 1)

                def down(j, par):
                    pe.wait_ge(hT_ready, j + 1)
                    if not (isinstance(j, int) and j == 0):
                        pe.wait_ge(low_ready, j)
                    for k in range(KD):
                        m = nc.tensor.matmul(ps_a[:, 0:AR], hT[:, k * P:(k + 1) * P], ar[:, k, :],
                                             start=(k == 0), stop=(k == KD - 1))
                    m.then_inc(a_done, 1)

                def dense(j, par):
                    if not (isinstance(j, int) and j == 0):
                        pe.wait_ge(y_ready, j)
                    for a, n in chunks(D):
                        for k in range(KD):
                            nc.tensor.matmul(ps_y[:, a:a + n], hT[:, k * P:(k + 1) * P], base[:, k, a:a + n],
                                             start=(k == 0), stop=False, skip_group_check=True)

                def low_transpose(j):
                    pe.wait_ge(low_ready, j + 1)
                    nc.tensor.transpose(ps_l[:, 0:P], low[:, :], ident[:, :]).then_inc(lowT_done, 1)

                def up(j, par):
                    if not top2 and not (isinstance(j, int) and j == 0):
                        pe.wait_ge(y_ready, j)
                    pe.wait_ge(lowT_ready, j + 1)
                    for a, n in chunks(D):
                        m = nc.tensor.matmul(ps_y[:, a:a + n], lowT[:, :], bT[:, a:a + n], start=not top2, stop=True,
                                             skip_group_check=True)
                    m.then_inc(y_done, 1)

                def step(j, par, first, last):
                    if not first:
                        low_transpose(j - 1)
                    if not last:
                        out_transposes(j + 1, 1 - par)
                    if not first:
                        up(j - 1, 1 - par)
                    if not last:
                        out_project(j + 1, 1 - par)
                    down(j, par)
                    if top2:
                        if first:
                            pe.wait_ge(base_in, 16)
                        dense(j, par)
                    if not last:
                        row_transposes(j + 1, 1 - par)

                pe.wait_ge(const_in, 16)
                out_transposes(0, 0)
                out_project(0, 0)
                row_transposes(0, 0)
                pe.wait_ge(rest_in, 16 * ab_loads)
                over_tiles(pe, step, 3)
                low_transpose(NT - 1)
                up(NT - 1, 1)

            @block.scalar
            def _(act):
                def evac(j, done, to, ready):
                    act.wait_ge(done, j + 1)
                    for a, n in chunks(D):
                        m = nc.scalar.copy(to[:, a:a + n], ps_t[:, a:a + n])
                    m.then_inc(ready, 1)

                def out_evac(j):
                    if not (isinstance(j, int) and j == 0):
                        act.wait_ge(wo_done, j * 2)
                    evac(j, oT_done, oT, oT_ready)

                def row_evac(j):
                    evac(j, hT_done, hT, hT_ready)

                def low_evac(j):
                    act.wait_ge(lowT_done, j + 1)
                    if not (isinstance(j, int) and j == 0):
                        act.wait_ge(y_done, j)
                    nc.scalar.copy(lowT[:, :], ps_l[:, 0:P]).then_inc(lowT_ready, 1)

                def step(j, par, first, last):
                    if not first:
                        low_evac(j - 1)
                    if not last:
                        out_evac(j + 1)
                    act.wait_ge(neg_ready, j + 1)
                    nc.scalar.activation(expd[:, :], logit[:, :], ACT.Exp, bias=neg[:, :],
                                         accum_out=total[:, :]).then_inc(exp_done, 1)
                    if not last:
                        row_evac(j + 1)

                out_evac(0)
                row_evac(0)
                over_tiles(act, step, 3)
                low_evac(NT - 1)

            @block.vector
            def _(dve):
                def residual(j, par):
                    dve.wait_ge(h_in[par], (j - par) * 8 + 16)
                    for n, (a, w) in enumerate(chunks(D)):
                        dve.wait_ge(wo_done, j * 2 + (n + 1))
                        m = nc.vector.tensor_tensor(h[:, par, a:a + w], ps_wo[:, a:a + w], h[:, par, a:a + w], ALU.add)
                        if n == 1:
                            m.then_inc(added, 1)
                        dve.drain()
                        if n == 1 and not (isinstance(j, int) and j == 0):
                            dve.wait_ge(hT_done, j)
                        nc.vector.bn_stats(stats[:, 6 * n:6 * n + 6], h[:, par, a:a + w])
                    layer_norm(nc, dve, h[:, par, :], stats[:, :], mv[:, :], rstd[:, :], hn[:, :],
                               False).then_inc(hn_ready, 1)

                def route(j, par):
                    dve.wait_ge(a_done, j + 1)
                    if top2:
                        nc.vector.tensor_copy(logit[:, :], ps_a[:, ER:AR])
                    else:
                        nc.vector.tensor_tensor(logit[:, :], ps_a[:, ER:AR], bias[:, 0:NE], ALU.add)
                    dve.drain()
                    nc.vector.tensor_reduce(top[:, :], logit[:, :], AX_X, ALU.max)
                    dve.drain()
                    nc.vector.tensor_scalar(neg[:, :], top[:, :], -1.0, None, ALU.mult).then_inc(neg_ready, 1)
                    dve.wait_ge(exp_done, j + 1)
                    if top2:
                        nc.vector.tensor_copy(weight[:, :], expd[:, :])
                        dve.drain()
                        nc.vector.max(best[:, :], weight[:, :])
                        dve.drain()
                        nc.vector.max_index(at[:, :], best[:, :], weight[:, :])
                        nc.vector.tensor_tensor(total[:, :], best[:, 0:1], best[:, 1:2], ALU.add)
                        dve.drain()
                        nc.vector.tensor_copy(at_f[:, :], at[:, 0:2])
                        nc.vector.reciprocal(inv[:, :], total[:, :])
                        dve.drain()
                        nc.vector.tensor_scalar(part[:, :], best[:, 0:2], inv[:, :], LORA, ALU.mult, ALU.mult)
                        dve.drain()
                        nc.vector.tensor_scalar(one[:, :], iota[:, :], at_f[:, 0:1], part[:, 0:1], ALU.is_equal,
                                                ALU.mult)
                        nc.vector.tensor_scalar(mix[:, :], iota[:, :], at_f[:, 1:2], part[:, 1:2], ALU.is_equal,
                                                ALU.mult)
                        dve.drain()
                        nc.vector.tensor_tensor(mix[:, :], mix[:, :], one[:, :], ALU.add)
                    else:
                        nc.vector.reciprocal(inv[:, :], total[:, :])
                        dve.drain()
                        nc.vector.tensor_scalar(mix[:, :], expd[:, :], inv[:, :], LORA * NE, ALU.mult, ALU.mult)
                    dve.drain()
                    if not (isinstance(j, int) and j == 0):
                        dve.wait_ge(lowT_done, j)
                    nc.vector.tensor_tensor(low[:, :].rearrange("p (e r) -> p e r", r=R),
                                            ps_a[:, 0:ER].rearrange("p (e r) -> p e r", r=R),
                                            mix[:, :].unsqueeze(2).to_broadcast([P, NE, R]),
                                            ALU.mult).then_inc(low_ready, 1)

                def finish(j, par):
                    if not (isinstance(j, int) and j < 2):
                        dve.wait_ge(y_out[par], (j - par) * 8)
                    if top2:
                        nc.vector.tensor_tensor(h[:, par, :], h[:, par, :], bias[:, :], ALU.add)
                        dve.drain()
                    dve.wait_ge(y_done, j + 1)
                    nc.vector.tensor_tensor(y[:, par, :], ps_y[:, :], h[:, par, :], ALU.add).then_inc(y_ready, 1)

                def step(j, par, first, last):
                    if not first:
                        finish(j - 1, 1 - par)
                    if not last:
                        residual(j + 1, 1 - par)
                    route(j, par)

                dve.wait_ge(rest_in, 16 * ab_loads)
                residual(0, 0)
                over_tiles(dve, step, 3)
                finish(NT - 1, 1)


def constants():
    import numpy as np
    from math import erf, sqrt

    inv_freq = (np.float32(1.0) / np.float32(10000.0) ** (np.arange(HALF, dtype=np.float32) / np.float32(HALF)))
    ang = np.arange(T, dtype=np.float32)[:, None] * inv_freq[None, :].astype(np.float32)
    cos, sin = np.cos(ang), np.sin(ang)
    rope = np.concatenate([cos, cos, -sin, sin], axis=1).astype(np.float32)
    rope = rope.reshape(TT, P, 2 * DH).transpose(1, 0, 2).reshape(P, TT * 2 * DH)
    causal = np.where(np.arange(P)[None, :] > np.arange(P)[:, None], MASKED, 0.0).astype(np.float32)
    row = np.arange(P)[:, None]
    tile = np.tile(np.arange(1, TT), 2)[None, :]
    keys = tile * P + row + 1
    share = np.clip(1 - AIM / keys, 0.02, 0.98)
    low, high = np.full(share.shape, -4.0), np.full(share.shape, 4.0)
    for _ in range(40):
        z = (low + high) / 2
        under = np.vectorize(lambda a: (1 + erf(a / sqrt(2))) / 2)(z) < share
        low, high = np.where(under, z, low), np.where(under, high, z)
    slope = keys * np.exp(-z * z / 2) / np.sqrt(2 * np.pi)
    columns = (tile + 1) * P + 0.0 * row
    search = np.stack([z, -0.5 / slope, columns - 2 * AIM, columns - 2 * keys, columns], axis=1)
    search = search.reshape(P, 5 * NS).astype(np.float32)
    iota = np.broadcast_to(np.arange(16, dtype=np.float32), (P, 16))
    return {"ident": np.eye(P, dtype=np.float32), "rope": np.ascontiguousarray(rope), "causal": causal,
            "search": np.ascontiguousarray(search), "iota": np.ascontiguousarray(iota)}


def build(nc, t, out, const):
    dram = lambda n, s, d=F32: nc.dram_tensor(n, s, d, kind="Internal").ap()
    h0, h1 = dram("h0", (B * T, D)), dram("h1", (B * T, D))
    qk0, v0, o0 = dram("qk0", (SPLITS * QK, B * T), BF16), dram("v0", (P, HKV * NT * DH)), dram("o0", (B * T, D))
    qk1, v1, o1 = dram("qk1", (SPLITS * QK, B * T), BF16), dram("v1", (P, HKV * NT * DH)), dram("o1", (B * T, D))
    with ExitStack() as ctx:
        w_in = [ctx.enter_context(nc.semaphore(f"w_in{k}")) for k in range(KD)]
        token_map(nc, t["ids"], t["embedding"], t["compat"], const, h0)
        project(nc, "p0_", w_in, 1, t["wqkv0"], const, h0, qk0, v0)
        attention(nc, const, qk0, v0, o0)
        mixture(nc, "m0_", w_in, 2, t["wo0"], t["ar0"], t["b0"], t["base"], t["base_bias"], const, h0, o0, h1)
        project(nc, "p1_", w_in, 3, t["wqkv1"], const, h1, qk1, v1)
        kept_attention(nc, const, qk1, v1, o1)
        mixture(nc, "m1_", w_in, 4, t["wo1"], t["ar1"], t["b1"], None, t["router_bias"], const, h1, o1, out)


def kernel(**inputs):
    import numpy as np
    import concourse.bacc as bacc
    from concourse.bass_utils import run_bass_kernel_spmd as run

    x = {k: np.asarray(v) for k, v in inputs.items()}
    arrays = {
        "ids": x["x"].reshape(NT, P).T,
        "embedding": x["L0_tok_dim_embedding"],
        "compat": x["L0_tok_compatibility"],
        "wqkv0": np.concatenate([x["L0_attn_Wq"], x["L0_attn_Wk"], x["L0_attn_Wv"]], axis=1),
        "wo0": x["L0_attn_Wo"],
        "ar0": np.concatenate([x["L0_ffn_A"].reshape(ER, D), x["L0_ffn_W_router"]], axis=0).T,
        "b0": x["L0_ffn_B"].transpose(0, 2, 1).reshape(ER, D),
        "base": x["L0_ffn_W_base"].T,
        "base_bias": x["L0_ffn_b_base"],
        "wqkv1": np.concatenate([x["L1_attn_Wq"], x["L1_attn_Wk"], x["L1_attn_Wv"]], axis=0).T,
        "wo1": x["L1_attn_Wo"].T,
        "ar1": np.concatenate([x["L1_ffn_A"].reshape(ER, D), x["L1_ffn_Wr"]], axis=0).T,
        "b1": x["L1_ffn_B"].transpose(0, 2, 1).reshape(ER, D),
        "router_bias": x["L1_ffn_br"],
    }
    consts = constants()
    nc = bacc.Bacc("TRN2", target_bir_lowering=False, num_devices=1)
    feed, taps, tabs = {}, {}, {}
    for group, aps in ((arrays, taps), (consts, tabs)):
        for name, a in group.items():
            a = np.ascontiguousarray(a)
            feed[f"in_{name}"] = a
            aps[name] = nc.dram_tensor(f"in_{name}", a.shape, mybir.dt.from_np(a.dtype), kind="ExternalInput").ap()
    out = nc.dram_tensor("out_0", (B, T, D), F32, kind="ExternalOutput").ap()
    build(nc, taps, out.rearrange("b t d -> (b t) d"), tabs)
    r = run(nc, [feed], core_ids=[0])
    return r.results[0]["out_0"]
```
